# Optimizing a Trainium2 kernel written in Bass

```python
import numpy as np
import jax
import jax.numpy as jnp

def _softmax(x, axis=-1):
    return jax.nn.softmax(x, axis=axis)

def _gelu(x):
    return jax.nn.gelu(x, approximate=True)

def _silu(x):
    return jax.nn.silu(x)

def _sigmoid(x):
    return jax.nn.sigmoid(x)

def _layernorm(x, axis=-1, eps=1e-05):
    m = jnp.mean(x, axis=axis, keepdims=True)
    v = jnp.var(x, axis=axis, keepdims=True)
    return (x - m) / jnp.sqrt(v + eps)

def _scatter_add(tgt, idx, src, axis=0):
    return tgt.at[idx].add(src)

def _segment_sum(src, seg, n):
    return jax.ops.segment_sum(src, seg, n)
kernel_name = 'mk_audio_tower_d1_tok_audfeat256_r4_027551'

def setup_inputs(seed: int=0):
    np.random.seed(seed)
    _w = jnp.asarray

    def _rec_inputs():
        import jax
        import jax.numpy as jnp
        _rk = jax.random.key(seed)
        x = -0.000520686 + 1.00062 * jax.random.normal(jax.random.fold_in(_rk, 1), (128, 375, 64), jnp.float32)
        return x
    x = _rec_inputs()

    def _L0_tok_setup():
        import jax, jax.numpy as jnp
        import numpy as np
        BATCH = 2
        SEQ = 1024
        D_MODEL = 64
        N_STATE = 64
        DT_RANK = 1
        NUM_LAYERS = 3

        def _ssm_layer(x, A_log, Dp, W_dbc, W_dt, b_dt):
            A = -jnp.exp(A_log)
            dbc = jnp.einsum('ble,ce->blc', x, W_dbc)
            delta, Bm, Cm = jnp.split(dbc, [DT_RANK, DT_RANK + N_STATE], axis=-1)
            delta = jax.nn.softplus(jnp.einsum('blr,er->ble', delta, W_dt) + b_dt)
            dA = jnp.exp(delta[..., None] * A)
            dBx = (delta * x)[..., None] * Bm[:, :, None, :]

            def combine(c1, c2):
                a1, h1 = c1
                a2, h2 = c2
                return (a1 * a2, h1 * a2 + h2)
            _, hs = jax.lax.associative_scan(combine, (dA, dBx), axis=1)
            y = jnp.einsum('blen,bln->ble', hs, Cm)
            return y + Dp * x
        key = jax.random.key(seed)
        kx, kw1, kw2 = jax.random.split(key, 3)
        x = jax.random.normal(kx, (BATCH, SEQ, D_MODEL), dtype=jnp.float32)
        A_log = jnp.broadcast_to(jnp.log(jnp.arange(1, N_STATE + 1, dtype=jnp.float32)), (NUM_LAYERS, D_MODEL, N_STATE)).copy()
        D = jnp.ones((NUM_LAYERS, D_MODEL), dtype=jnp.float32)
        W_dbc = 0.02 * jax.random.normal(kw1, (NUM_LAYERS, DT_RANK + 2 * N_STATE, D_MODEL), dtype=jnp.float32)
        W_dt = 0.02 * jax.random.normal(kw2, (NUM_LAYERS, D_MODEL, DT_RANK), dtype=jnp.float32)
        b_dt = jnp.zeros((NUM_LAYERS, D_MODEL), dtype=jnp.float32)
        return {'x': x, 'A_log': A_log, 'D': D, 'W_dbc': W_dbc, 'W_dt': W_dt, 'b_dt': b_dt}
    _L0_tok_all = _L0_tok_setup()
    _L0_tok_in = {k: v for k, v in _L0_tok_all.items() if k in ('A_log', 'D', 'W_dbc', 'W_dt', 'b_dt')}
    del _L0_tok_all

    def _L0_attn_setup():
        import jax, jax.numpy as jnp
        import numpy as np
        B_SZ, L, H, P = (16, 256, 64, 64)
        DT_MIN, DT_MAX = (0.001, 0.1)

        def _binop(ei, ej):
            ai, bi = ei
            aj, bj = ej
            return (aj * ai, aj * bi + bj)
        key = jax.random.key(seed)
        ks = jax.random.split(key, 6)
        u = jax.random.normal(ks[0], (B_SZ, L, H), dtype=jnp.float32)
        Lambda_re = -0.5 * jnp.ones((P,), jnp.float32)
        Lambda_im = jnp.pi * jnp.arange(P, dtype=jnp.float32)
        Bp = jax.random.normal(ks[1], (P, H, 2), jnp.float32) / jnp.sqrt(2.0 * H)
        Cp = jax.random.normal(ks[2], (H, P, 2), jnp.float32) / jnp.sqrt(2.0 * P)
        D = jax.random.normal(ks[3], (H,), jnp.float32)
        log_step = jax.random.uniform(ks[4], (P, 1), jnp.float32) * (jnp.log(DT_MAX) - jnp.log(DT_MIN)) + jnp.log(DT_MIN)
        return {'u': u, 'Lambda_re': Lambda_re, 'Lambda_im': Lambda_im, 'B': Bp, 'C': Cp, 'D': D, 'log_step': log_step}
    _L0_attn_all = _L0_attn_setup()
    _L0_attn_in = {k: v for k, v in _L0_attn_all.items() if k in ('Lambda_re', 'Lambda_im', 'B', 'C', 'D', 'log_step')}
    del _L0_attn_all

    def _L0_ffn_setup():
        import jax, jax.numpy as jnp
        import numpy as np
        B, K, D = (128, 16, 64)
        E = 32
        H = int(D * 0.25)
        key = jax.random.key(seed)
        ks = jax.random.split(key, 7)
        d_rs = D ** (-0.5)
        h_rs = H ** (-0.5)
        x = jax.random.normal(ks[0], (B, K, D), dtype=jnp.float32)
        router_w = jax.random.uniform(ks[1], (E, D), jnp.float32, -d_rs, d_rs)
        router_b = jax.random.uniform(ks[2], (E,), jnp.float32, -d_rs, d_rs)
        W1 = jax.random.uniform(ks[3], (E, D, H), jnp.float32, -h_rs, h_rs)
        b1 = jax.random.uniform(ks[4], (E, H), jnp.float32, -h_rs, h_rs)
        W2 = jax.random.uniform(ks[5], (E, H, D), jnp.float32, -d_rs, d_rs)
        b2 = jax.random.uniform(ks[6], (E, D), jnp.float32, -d_rs, d_rs)
        return {'x': x, 'router_w': router_w, 'router_b': router_b, 'W1': W1, 'b1': b1, 'W2': W2, 'b2': b2}
    _L0_ffn_all = _L0_ffn_setup()
    _L0_ffn_in = {k: v for k, v in _L0_ffn_all.items() if k in ('router_w', 'router_b', 'W1', 'b1', 'W2', 'b2')}
    del _L0_ffn_all
    return {'x': x, 'L0_tok_A_log': _L0_tok_in['A_log'], 'L0_tok_D': _L0_tok_in['D'], 'L0_tok_W_dbc': _L0_tok_in['W_dbc'], 'L0_tok_W_dt': _L0_tok_in['W_dt'], 'L0_tok_b_dt': _L0_tok_in['b_dt'], 'L0_attn_Lambda_re': _L0_attn_in['Lambda_re'], 'L0_attn_Lambda_im': _L0_attn_in['Lambda_im'], 'L0_attn_B': _L0_attn_in['B'], 'L0_attn_C': _L0_attn_in['C'], 'L0_attn_D': _L0_attn_in['D'], 'L0_attn_log_step': _L0_attn_in['log_step'], 'L0_ffn_router_w': _L0_ffn_in['router_w'], 'L0_ffn_router_b': _L0_ffn_in['router_b'], 'L0_ffn_W1': _L0_ffn_in['W1'], 'L0_ffn_b1': _L0_ffn_in['b1'], 'L0_ffn_W2': _L0_ffn_in['W2'], 'L0_ffn_b2': _L0_ffn_in['b2']}

def reference(x, L0_tok_A_log, L0_tok_D, L0_tok_W_dbc, L0_tok_W_dt, L0_tok_b_dt, L0_attn_Lambda_re, L0_attn_Lambda_im, L0_attn_B, L0_attn_C, L0_attn_D, L0_attn_log_step, L0_ffn_router_w, L0_ffn_router_b, L0_ffn_W1, L0_ffn_b1, L0_ffn_W2, L0_ffn_b2):
    import jax
    import jax.numpy as jnp

    def _L0_tok_ref(x, A_log, D, W_dbc, W_dt, b_dt):
        import jax, jax.numpy as jnp
        import numpy as np
        BATCH = 2
        SEQ = 1024
        D_MODEL = 64
        N_STATE = 64
        DT_RANK = 1
        NUM_LAYERS = 3

        def _ssm_layer(x, A_log, Dp, W_dbc, W_dt, b_dt):
            A = -jnp.exp(A_log)
            dbc = jnp.einsum('ble,ce->blc', x, W_dbc)
            delta, Bm, Cm = jnp.split(dbc, [DT_RANK, DT_RANK + N_STATE], axis=-1)
            delta = jax.nn.softplus(jnp.einsum('blr,er->ble', delta, W_dt) + b_dt)
            dA = jnp.exp(delta[..., None] * A)
            dBx = (delta * x)[..., None] * Bm[:, :, None, :]

            def combine(c1, c2):
                a1, h1 = c1
                a2, h2 = c2
                return (a1 * a2, h1 * a2 + h2)
            _, hs = jax.lax.associative_scan(combine, (dA, dBx), axis=1)
            y = jnp.einsum('blen,bln->ble', hs, Cm)
            return y + Dp * x
        for i in range(NUM_LAYERS):
            x = _ssm_layer(x, A_log[i], D[i], W_dbc[i], W_dt[i], b_dt[i])
            if i < NUM_LAYERS - 1:
                b, l, d = x.shape
                x = x[:, :l // 2 * 2].reshape(b, l // 2, 2, d).mean(axis=2)
        return x

    def _L0_attn_ref(u, Lambda_re, Lambda_im, B, C, D, log_step):
        import jax, jax.numpy as jnp
        import numpy as np
        B_SZ, L, H, P = (16, 256, 64, 64)
        DT_MIN, DT_MAX = (0.001, 0.1)

        def _binop(ei, ej):
            ai, bi = ei
            aj, bj = ej
            return (aj * ai, aj * bi + bj)
        Lambda = Lambda_re + 1j * Lambda_im
        B_tilde = B[..., 0] + 1j * B[..., 1]
        C_tilde = C[..., 0] + 1j * C[..., 1]
        Delta = jnp.exp(log_step[:, 0])
        Lambda_bar = jnp.exp(Lambda * Delta)
        B_bar = ((Lambda_bar - 1.0) / Lambda)[:, None] * B_tilde
        Bu = jnp.einsum('ph,blh->blp', B_bar, u.astype(B_bar.dtype))
        Lam = jnp.broadcast_to(Lambda_bar, Bu.shape)
        _, xs = jax.lax.associative_scan(_binop, (Lam, Bu), axis=1)
        ys = 2.0 * jnp.einsum('hp,blp->blh', C_tilde, xs).real
        return ys + D * u

    def _L0_ffn_ref(x, router_w, router_b, W1, b1, W2, b2):
        import jax, jax.numpy as jnp
        import numpy as np
        B, K, D = (128, 16, 64)
        E = 32
        H = int(D * 0.25)
        xf = x.reshape(-1, D)
        logits = xf @ router_w.T + router_b
        idx = jnp.argmax(logits, axis=-1)
        w1t = jnp.take(W1, idx, axis=0)
        h = jnp.einsum('nd,ndh->nh', xf, w1t) + jnp.take(b1, idx, axis=0)
        h = jax.nn.relu(h)
        w2t = jnp.take(W2, idx, axis=0)
        out = jnp.einsum('nh,nhd->nd', h, w2t) + jnp.take(b2, idx, axis=0)
        out = jax.nn.relu(out)
        return out.reshape(x.shape)
    h = _L0_tok_ref(x, L0_tok_A_log, L0_tok_D, L0_tok_W_dbc, L0_tok_W_dt, L0_tok_b_dt)
    h = h + _L0_attn_ref(_layernorm(h, axis=-1), L0_attn_Lambda_re, L0_attn_Lambda_im, L0_attn_B, L0_attn_C, L0_attn_D, L0_attn_log_step)
    h = h + _L0_ffn_ref(_layernorm(h, axis=-1), L0_ffn_router_w, L0_ffn_router_b, L0_ffn_W1, L0_ffn_b1, L0_ffn_W2, L0_ffn_b2)
    return h

_drawn_inputs = setup_inputs


def setup_inputs(seed=0):
    import zlib

    import numpy as np

    out = dict(_drawn_inputs(seed))
    spreads = {'L0_tok_D': (1.0, 0.2), 'L0_tok_b_dt': (0.0, 0.37), 'L0_attn_Lambda_re': (-0.5, 0.6)}
    factors = {'L0_tok_A_log': 11.594, 'L0_tok_W_dt': 49.625, 'L0_ffn_b1': 3.786}
    for name, (base, spread) in spreads.items():
        noise = np.random.default_rng([zlib.crc32(name.encode()), seed]).standard_normal(out[name].shape)
        drawn = base * np.exp(spread * noise) if base else spread * noise
        out[name] = jnp.asarray(drawn.astype(out[name].dtype))
    for name, factor in factors.items():
        out[name] = (out[name] * factor).astype(out[name].dtype)
    return out
```

```python
import concourse.bass as bass
from concourse import mybir
from contextlib import ExitStack

FP32 = mybir.dt.float32
BF16 = mybir.dt.bfloat16
ALU = mybir.AluOpType
ACT = mybir.ActivationFunctionType

D = 64
NS = 64
P = 128
LAYERS = 3
LENGTHS = (372, 186, 93)
SEQS_MAX = 2 * LENGTHS[0] // LENGTHS[-1]
UNIT = LENGTHS[0]
W = 2 * UNIT
BANK = 512
STEPS = D
RING = 4
BLOCKS = STEPS // RING
REPEATED = (1, 2)
LAG = RING
EXPS_ON_JOINT_TABLE = 6
PREP_ITEMS = ("dt", "B", "C")
ITEM_SLOTS = len(PREP_ITEMS)
PARTS = 3
QR = 32
NQ = P // QR
EPQ = D // NQ

HALVES = ((0, BANK), (BANK, W))


def known_below(n, limit):
    return isinstance(n, int) and n < limit


def ssm_stage(nc, io, h3, n_batch):
    groups = [n_batch * LENGTHS[l] // (2 * W) for l in range(LAYERS)]
    pair_mean = [True, True, False]

    step0, slot0, sum0, prep0 = [0], [0], [0], [0]
    for g in groups:
        step0.append(step0[-1] + STEPS * g + LAG)
        slot0.append(slot0[-1] + ITEM_SLOTS + (STEPS + ITEM_SLOTS) * g + LAG)
        sum0.append(sum0[-1] + BLOCKS * g)
        prep0.append(prep0[-1] + g + 1)
    group0 = [0]
    for g in groups:
        group0.append(group0[-1] + g)
    ITEM_AFTER = (11, 15, 19)

    def step(l, g, e):
        return step0[l] + STEPS * g + e

    def slot(l, g, e, past=0):
        return slot0[l] + ITEM_SLOTS + (STEPS + ITEM_SLOTS) * g + e + past

    def item_slot(l, p, i):
        if isinstance(p, int) and p == 0:
            return slot0[l] + i
        return slot(l, p - 1, ITEM_AFTER[i] + 1, i)

    def odd_slot(l, half, r, past):
        return (slot0[l] + ITEM_SLOTS + (STEPS + ITEM_SLOTS) * half + r + past) % 2

    def odd_item(l, buf, i):
        return odd_slot(l, 1 - buf, ITEM_AFTER[i] + 1, i)

    def users():
        for e in range(STEPS):
            yield "step", e
            if e in ITEM_AFTER:
                yield "item", ITEM_AFTER.index(e)

    def done(n):
        return n + 2

    ctx = ExitStack()
    with ctx:
        def sb(name, shape, dt=FP32):
            return ctx.enter_context(nc.sbuf_tensor(name, shape, dt))

        def ps(name):
            return ctx.enter_context(nc.psum_tensor(name, [P, 2 * BANK], FP32))

        def sem(name):
            return ctx.enter_context(nc.semaphore(name))

        wdt = sb("w_dt_rows", [P, LAYERS, P])
        wB = sb("w_B_rows", [P, LAYERS, P])
        wC = sb("w_C_rows", [P, LAYERS, P])
        a_log = sb("a_log", [P, LAYERS, D])
        a_neg = sb("a_neg", [P, LAYERS, D])
        cols = sb("cols", [P, 3 * LAYERS])
        d_out = sb("d_out", [P, LAYERS])
        spread_f = sb("spread_f", [P, EPQ * P])
        spread = sb("spread", [P, EPQ, P], BF16)
        gather = sb("gather", [P, 2, 2 * QR - 2])
        xT = [sb(f"xT{i}", [P, W]) for i in range(2)]
        Bt = [sb(f"Bt{i}", [P, W]) for i in range(2)]
        Ct = [sb(f"Ct{i}", [P, W]) for i in range(2)]
        stk_delta = [sb(f"stk_delta{i}", [P, NQ, W], BF16) for i in range(2)]
        stk_dx = [sb(f"stk_dx{i}", [P, NQ, W], BF16) for i in range(2)]
        parts_delta = sb("parts_delta", [P, PARTS, W], BF16)
        parts_dx = sb("parts_dx", [P, PARTS, W], BF16)
        u = [sb(f"u{i}", [P, W]) for i in range(RING)]
        zero = sb("zero", [P, SEQS_MAX])
        h = [sb(f"h_slot{i}", [P, W]) for i in range(RING)]
        hC = [sb(f"hC{i}", [P, W]) for i in range(2 * RING)]
        t_v, t_abs, t_relu, t_w, t_ln = sb("t_v", [P, W]), sb("t_abs", [P, W]), sb("t_relu", [P, W]), sb("t_w", [P, W]), sb("t_ln", [P, W])
        t_one, t_sum, delta, dx = sb("t_one", [P, W]), sb("t_sum", [P, W]), sb("delta", [P, W]), sb("dx", [P, W])
        y_full, y_out = sb("y_full", [P, W]), sb("y_out", [P, W])
        db = [ps(f"decay_bank{i}") for i in range(2)]
        xb, y = ps("dx_bank"), ps("y")

        def row(t):
            return t[:, 0:W]

        s_const = sem("constants_loaded")
        s_cast = sem("spread_cast")
        s_rows = sem("spare_rows_zeroed")
        s_dout = sem("d_out_ready")
        s_aexp, s_aneg = sem("a_exp"), sem("a_neg_ready")
        s_zero = sem("zero_set")
        s_x = sem("x_loaded")
        s_stkd, s_stkx = sem("stk_delta_loaded"), sem("stk_dx_loaded")
        s_dbw, s_dbr = sem("decay_bank_written"), sem("decay_bank_read")
        s_read = sem("item_read")
        s_xbw, s_u, s_scan = sem("dx_bank_written"), sem("u_done"), sem("scan_done")
        s_hC, s_sum = sem("hC_done"), sem("summed")
        s_abs, s_w, s_ln = sem("abs_done"), sem("w_done"), sem("ln_done")
        s_one, s_c, s_s = sem("one_done"), sem("rest_done"), sem("log1p_done")
        s_delta, s_dx = sem("delta_done"), sem("dx_done")
        s_hd, s_rd, s_md, s_ld = sem("delta_hi"), sem("delta_rest"), sem("delta_mid"), sem("delta_lo")
        s_hx, s_rx, s_mx, s_lx = sem("dx_hi"), sem("dx_rest"), sem("dx_mid"), sem("dx_lo")
        s_turn = sem("store_turn")
        s_post, s_yout, s_store = sem("y_taken"), sem("y_out_done"), sem("y_stored")
        block = ctx.enter_context(nc.Block())
        N_CONST = 7

        def by_sequence(l, t):
            return row(t).rearrange("p (s t) -> p s t", t=LENGTHS[l])

        def after_firsts(l):
            T = LENGTHS[l]
            whole, cut = divmod(BANK, T)
            return ((0, whole, 1, T), (whole, 1, 1, cut), (whole, 1, cut, T)) + (
                ((whole + 1, W // T - whole - 1, 1, T),) if W // T > whole + 1 else ())

        def layer_loop(eng, l, prologue, half_body):
            prologue(l)
            with eng.Fori(0, groups[l] // 2) as k:
                for half in range(2):
                    half_body(l, 2 * k + half, half)

        @block.sync
        def _(sp):
            sp.sem_inc(s_store, 1)
            for dst, src in ((wdt, io["wdt"]), (wB, io["wB"]), (wC, io["wC"]), (a_log, io["a_log"]), (gather, io["gather"])):
                sp.dma_start(dst[:, :, :], src.rearrange("l p m -> p l m")).then_inc(s_const, 16)
            sp.dma_start(cols[:, :], io["cols"]).then_inc(s_const, 16)
            sp.dma_start(spread_f[:, :], io["spread"]).then_inc(s_const, 16)

            def load_x(l, p, buf):
                src = io["x"][:, bass.ds(p * W, W)] if l == 0 else h3[:, bass.ds(p * W, W)]
                sp.dma_start(xT[buf][:, :], src).then_inc(s_x, 16)

            def stack(prep, buf):
                for ready, loaded, stk, parts in ((s_ld, s_stkd, stk_delta, parts_delta), (s_lx, s_stkx, stk_dx, parts_dx)):
                    sp.wait_ge(ready, prep)
                    for q in range(NQ):
                        for part in range(PARTS):
                            sp.dma_start(stk[buf][QR * part:QR * part + QR, q, :],
                                         parts[QR * q:QR * q + QR, part, :]).then_inc(loaded, 16)

            def prologue(l):
                if l > 0:
                    sp.wait_ge(s_store, 16 * group0[l] + 1)
                    sp.wait_ge(s_dx, prep0[l])
                    sp.wait_ge(s_dbr, done(slot0[l] - 1))
                    sp.wait_ge(s_xbw, done(step0[l] - 1))
                load_x(l, 0, 0)
                stack(prep0[l] + 1, 0)

            def half_body(l, g, half):
                n = W // 2 if pair_mean[l] else W
                outputs, prep = group0[l] + g + 1, prep0[l] + g + 2
                sp.wait_ge(s_post, outputs)
                load_x(l, g + 1, 1 - half)
                stack(prep, 1 - half)
                if pair_mean[l]:
                    sp.wait_ge(s_yout, outputs)
                else:
                    sp.wait_ge(s_post, outputs + 1)
                sp.sem_inc(s_turn, 1)
                sp.dma_start(h3[:, bass.ds(g * n, n)], y_out[:, 0:n]).then_inc(s_store, 16)

            for l in range(LAYERS):
                layer_loop(sp, l, prologue, half_body)
            sp.wait_ge(s_store, 16 * group0[LAYERS] + 1)

        @block.tensor
        def _(pe):
            pe.sem_inc(s_dbw, 1)
            pe.sem_inc(s_xbw, 1)
            pe.sem_inc(s_sum, 1)
            pe.wait_ge(s_const, 16 * N_CONST)
            pe.wait_ge(s_cast, 1)
            pe.wait_ge(s_rows, 4)

            def wait_slot(l, g, k):
                if k >= 2:
                    (kind, n), ahead = order[k - 2], 0
                elif isinstance(g, int) and g == 0:
                    kind, n = "item", k + 1
                    pe.wait_ge(s_dbr, done(item_slot(l, 0, n)))
                    return
                else:
                    (kind, n), ahead = order[k - 2], 1
                if kind == "step":
                    pe.wait_ge(s_scan, done(step(l, g - ahead, n)))
                else:
                    pe.wait_ge(s_dbr, done(item_slot(l, g + 1, n)))

            order = list(users())

            def item(l, p, buf, i):
                pe.wait_ge(s_x, 16 * (prep0[l] + p + 1))
                if not (isinstance(p, int) and p == 0):
                    wait_slot(l, p - 1, order.index(("item", i)))
                elif i == 2:
                    pe.wait_ge(s_dbr, done(item_slot(l, 0, 0)))
                elif l:
                    pe.wait_ge(s_scan, done(step0[l] - 2 + i))
                wt = (wdt, wB, wC)[i]
                for lo, hi in HALVES:
                    last = nc.tensor.matmul(db[odd_item(l, buf, i)][:, lo:hi], wt[:, l, :], xT[buf][:, lo:hi],
                                            start=True, stop=True)
                last.then_inc(s_dbw, 1)

            def spread_dx(l, g, buf, e):
                j, q = divmod(e, RING)
                if e == 0:
                    pe.wait_ge(s_stkx, 16 * NQ * PARTS * (prep0[l] + g + 1))
                if not known_below(step(l, g, e), 1):
                    pe.wait_ge(s_u, done(step(l, g, e) - 1))
                for lo, hi in ((HALVES[0], *HALVES) if q in REPEATED else HALVES):
                    last = nc.tensor.matmul(xb[:, lo:hi], spread[:, j, :], stk_dx[buf][:, q, lo:hi],
                                            start=True, stop=True)
                last.then_inc(s_xbw, 1)

            def spread_delta(l, g, buf, e, past):
                j, q = divmod(e, RING)
                if e == 0:
                    pe.wait_ge(s_stkd, 16 * NQ * PARTS * (prep0[l] + g + 1))
                wait_slot(l, g, order.index(("step", e)))
                bank = by_sequence(l, db[odd_slot(l, buf, e, past)])
                stk = stk_delta[buf][:, q, :].rearrange("p (s t) -> p s t", t=LENGTHS[l])
                pieces = after_firsts(l)
                for s, n, lo, hi in pieces * 2 if q in REPEATED else pieces:
                    last = nc.tensor.matmul(bank[:, s:s + n, lo:hi], spread[:, j, :], stk[:, s:s + n, lo:hi],
                                            start=True, stop=True)
                last.then_inc(s_dbw, 1)

            def sum_block(l, g, j, bank):
                a, z = HALVES[bank]
                if bank == 0:
                    if j == 0:
                        pe.wait_ge(s_post, group0[l] + g + 1)
                    pe.wait_ge(s_hC, done(step(l, g, RING * j + RING - 1)))
                lo = 2 * (EPQ - 1 - j)
                for q in range(NQ):
                    last = nc.tensor.matmul(y[QR * q:QR * (q + 1), a:z], gather[:, 0 if pair_mean[l] else 1, lo:lo + QR],
                                            hC[RING * (j % 2) + q][:, a:z], start=(j == 0), stop=(j == BLOCKS - 1),
                                            tile_position=(0, QR * q))
                if bank == 1:
                    last.then_inc(s_sum, 1)

            def prologue(l):
                for i in range(ITEM_SLOTS):
                    item(l, 0, 0, i)
                for e in range(LAG):
                    spread_dx(l, 0, 0, e)
                    spread_delta(l, 0, 0, e, 0)

            def half_body(l, g, half):
                past = 0
                for n in range(LAG, STEPS + LAG):
                    at = (l, g, half, n) if n < STEPS else (l, g + 1, 1 - half, n - STEPS)
                    last_of_block = n % RING == RING - 1
                    if n - 2 not in ITEM_AFTER:
                        spread_dx(*at)
                    if n - 1 in ITEM_AFTER:
                        item(l, g + 1, 1 - half, past)
                        past += 1
                        spread_dx(l, g, half, n + 1)
                    if last_of_block:
                        sum_block(l, g, n // RING - 1, 0)
                    spread_delta(*at, past if n < STEPS else 0)
                    if last_of_block:
                        sum_block(l, g, n // RING - 1, 1)

            for l in range(LAYERS):
                layer_loop(pe, l, prologue, half_body)

        SINGLE = 10

        def half_steps(eng, l, g, half, step_block, between):
            for j in range(1, SINGLE):
                step_block(l, g, half, j, j % 2, min(max(j - 2, 0), ITEM_SLOTS))
                if between and j >= 2:
                    between(l, g + 1, 1 - half, j - 2)
            with eng.Fori(SINGLE // 2, BLOCKS // 2) as pair:
                for odd in range(2):
                    step_block(l, g, half, 2 * pair + odd, odd, ITEM_SLOTS)
            step_block(l, g + 1, 1 - half, 0, 0, 0)

        @block.scalar
        def _(act):
            nc.scalar.add_instruction(mybir.InstLoadActFuncSet(
                name=nc.get_next_instruction_name(), engine=mybir.EngineType.Activation, ins=[], outs=[],
                act_func_set_id=EXPS_ON_JOINT_TABLE))
            act.sem_inc(s_dbr, 1)
            act.wait_ge(s_const, 16 * N_CONST)
            nc.scalar.activation(a_log[:, :, :], a_log[:, :, :], ACT.Exp).then_inc(s_aexp, 1)
            act.wait_ge(s_aexp, 1)
            nc.scalar.mul(a_neg[:, :, :], a_log[:, :, :], -1.0).then_inc(s_aneg, 1)
            act.wait_ge(s_aneg, 1)
            act.wait_ge(s_zero, 1)

            def step_block(l, g, half, j, odd, past):
                for r in range(RING):
                    e = RING * j + r
                    act.wait_ge(s_dbw, done(slot(l, g, e, past)))
                    bank = by_sequence(l, db[odd_slot(l, half, r, past)])[:, :, 1:]
                    nc.scalar.activation(bank, bank, ACT.Exp, scale=a_neg[:, l, bass.ds(e, 1)]).then_inc(s_dbr, 1)
                    if isinstance(j, int) and j >= 3:
                        beside(l, g + 1, j - 3, r)

            def clear_firsts(l, bank, k):
                act.wait_ge(s_read, k + 1)
                nc.scalar.copy(by_sequence(l, bank)[:, :, 0:1], zero[:, 0:W // LENGTHS[l]].unsqueeze(2)).then_inc(s_dbr, 1)

            def item(l, p, buf, i):
                act.wait_ge(s_dbw, done(item_slot(l, p, i)))
                n = prep0[l] + p
                bank = db[odd_item(l, buf, i)]
                if i == 0:
                    if not known_below(n, 1):
                        act.wait_ge(s_delta, n)
                    sc, bi = cols[:, 3 * l:3 * l + 1], cols[:, 3 * l + 1:3 * l + 2]
                    nc.scalar.activation(t_v[:, :], row(bank), ACT.Identity, scale=sc, bias=bi).then_inc(s_read, 1)
                    clear_firsts(l, bank, ITEM_SLOTS * n)
                elif i == 1:
                    nc.scalar.copy(Bt[buf][:, :], row(bank)).then_inc(s_read, 1)
                    clear_firsts(l, bank, ITEM_SLOTS * n + 1)
                else:
                    act.wait_ge(s_hC, done(step(l, p - 1, 0) - 1) if not known_below(p, 1)
                                else done(step0[l] - 1) if l else 1)
                    nc.scalar.copy(Ct[buf][:, :], row(bank)).then_inc(s_read, 1)
                    clear_firsts(l, bank, ITEM_SLOTS * n + 2)

            def softplus(n, part):
                if part == 0:
                    act.wait_ge(s_read, ITEM_SLOTS * n + 1)
                    nc.scalar.activation(t_abs[:, :], t_v[:, :], ACT.Abs).then_inc(s_abs, 1)
                if part == 1:
                    nc.scalar.activation(t_relu[:, :], t_v[:, :], ACT.Relu)
                if part == 2:
                    act.wait_ge(s_abs, n + 1)
                    nc.scalar.activation(t_w[:, :], t_abs[:, :], ACT.Exp, scale=-1.0).then_inc(s_w, 1)
                if part == 3:
                    act.wait_ge(s_w, n + 1)
                    nc.scalar.activation(t_abs[:, :], t_w[:, :], ACT.Identity, bias=1.0).then_inc(s_one, 1)
                if part == 4:
                    nc.scalar.activation(t_ln[:, :], t_w[:, :], ACT.Ln, bias=1.0).then_inc(s_ln, 1)

            def beside(l, p, n, r):
                k = prep0[l] + p
                if n == 0:
                    softplus(k, r)
                if n == 1 and r == 0:
                    softplus(k, RING)
                if n == 4 and r == 1:
                    cast(dx, s_dx, parts_dx, 0, s_hx, s_stkx, k)

            def cast(src, src_sem, dst, part, dst_sem, loaded, n):
                act.wait_ge(src_sem, n + 1)
                if part == 0 and not known_below(n, 1):
                    act.wait_ge(loaded, 16 * NQ * PARTS * n)
                nc.scalar.copy(dst[:, part, :], src[:, :]).then_inc(dst_sem, 1)

            def between(l, p, buf, n):
                k = prep0[l] + p
                if n < ITEM_SLOTS:
                    item(l, p, buf, n)
                if n == 4:
                    cast(delta, s_delta, parts_delta, 0, s_hd, s_stkd, k)
                if n == 5:
                    cast(t_sum, s_rd, parts_delta, 1, s_md, s_stkd, k)
                if n == 6:
                    cast(t_one, s_rx, parts_dx, 1, s_mx, s_stkx, k)

            def prologue(l):
                if l > 0:
                    act.wait_ge(s_u, done(step0[l] - 1))
                for n in range(SINGLE - 2):
                    between(l, 0, 0, n)
                    for r in range(RING):
                        beside(l, 0, n, r)
                step_block(l, 0, 0, 0, 0, 0)

            def half_body(l, g, half):
                half_steps(act, l, g, half, step_block, between)

            for l in range(LAYERS):
                layer_loop(act, l, prologue, half_body)

        @block.vector
        def _(dve):
            tt, stt = nc.vector.tensor_tensor, nc.vector.scalar_tensor_tensor
            dve.sem_inc(s_u, 1)
            dve.sem_inc(s_scan, 1)
            dve.sem_inc(s_post, 1)
            nc.vector.memset(zero[:, :], 0.0).then_inc(s_zero, 1)
            for stk in (*stk_delta, *stk_dx):
                nc.vector.memset(stk[PARTS * QR:P, :, :], 0.0).then_inc(s_rows, 1)
            dve.wait_ge(s_const, 16 * N_CONST)
            nc.vector.tensor_copy(spread[:, :, :], spread_f[:, :].rearrange("p (r m) -> p r m", r=EPQ)).then_inc(s_cast, 1)
            for l in range(LAYERS):
                last = nc.vector.tensor_scalar(d_out[:, l:l + 1], cols[:, 3 * l + 2:3 * l + 3],
                                               0.5 if pair_mean[l] else 1.0, None, ALU.mult)
            last.then_inc(s_dout, 1)
            nc.vector.memset(h3[:, groups[1] * W:(groups[1] + 1) * W], 0.0).then_inc(s_dout, 1)
            dve.wait_ge(s_dout, 2)

            def multiply(l, g, half, e, r):
                dve.wait_ge(s_xbw, done(step(l, g, e)))
                tt(u[r][:, :], row(xb), Bt[half][:, :], ALU.mult).then_inc(s_u, 1)

            def scan(l, n, dA_slot, bank, r):
                if not known_below(n, RING):
                    dve.wait_ge(s_hC, done(n - RING))
                dve.wait_ge(s_u, done(n))
                dve.wait_ge(s_dbr, done(dA_slot))
                nc.vector.tensor_tensor_scan(h[r][:, :], row(db[bank]), u[r][:, :], 0.0,
                                             ALU.mult, ALU.add).then_inc(s_scan, 1)

            def step_block(l, g, half, j, odd, past):
                if known_below(j, 1):
                    dve.wait_ge(s_dbr, done(item_slot(l, g, 1)))
                item_between = isinstance(j, int) and RING * j - 1 in ITEM_AFTER
                for r in range(RING):
                    e = RING * j + r
                    multiply(l, g, half, e, r)
                    if r or not (known_below(g, 1) and known_below(j, 1)):
                        back = 2 if item_between and r == 0 else 1
                        scan(l, step(l, g, e) - 1, slot(l, g, e, past) - back,
                             (odd_slot(l, half, r, past) - back) % 2, (r - 1) % RING)
                    if r == 0 and isinstance(j, int) and j >= 3:
                        prepare(l, g + 1, j - 3)

            def last_scan(l):
                e = RING - 1
                scan(l, step(l, groups[l], e), slot(l, groups[l], e), odd_slot(l, 0, e, 0), e)

            def split(out, a, b, ready, k, signal):
                dve.wait_ge(ready, k + 1)
                tt(out, a, b, ALU.subtract).then_inc(signal, 1)

            def prepare(l, p, n):
                k = prep0[l] + p
                if n == 1:
                    dve.wait_ge(s_one, k + 1)
                    stt(t_one[:, :], t_abs[:, :], 1.0, t_w[:, :], ALU.subtract, ALU.subtract).then_inc(s_c, 1)
                if n == 2:
                    dve.wait_ge(s_ln, k + 1)
                    split(t_sum[:, :], t_ln[:, :], t_one[:, :], s_c, k, s_s)
                if n == 4:
                    split(t_sum[:, :], delta[:, :], parts_delta[:, 0, :], s_hd, k, s_rd)
                if n == 5:
                    split(t_one[:, :], dx[:, :], parts_dx[:, 0, :], s_hx, k, s_rx)
                if n == 6:
                    split(parts_delta[:, 2, :], t_sum[:, :], parts_delta[:, 1, :], s_md, k, s_ld)
                    split(parts_dx[:, 2, :], t_one[:, :], parts_dx[:, 1, :], s_mx, k, s_lx)

            def prologue(l):
                if l > 0:
                    dve.wait_ge(s_scan, done(step0[l] - 1))
                for n in range(SINGLE - 3):
                    prepare(l, 0, n)
                step_block(l, 0, 0, 0, 0, 0)

            def half_body(l, g, half):
                half_steps(dve, l, g, half, step_block, None)
                m = group0[l] + g
                if pair_mean[l]:
                    out = y_full
                    if not known_below(m, 1):
                        dve.wait_ge(s_yout, m)
                else:
                    out = y_out
                    dve.wait_ge(s_store, 16 * m + 1)
                dve.wait_ge(s_sum, done(sum0[l] + BLOCKS * (g + 1) - 1))
                stt(out[:, :], xT[half][:, :], d_out[:, l:l + 1], row(y), ALU.mult, ALU.add).then_inc(s_post, 1)

            for l in range(LAYERS):
                layer_loop(dve, l, prologue, half_body)
                last_scan(l)

        @block.gpsimd
        def _(pool):
            pool.sem_inc(s_hC, 1)

            def step_block(l, g, half, j, odd, past):
                if isinstance(j, int) and j == 0:
                    pool.wait_ge(s_dbr, done(item_slot(l, g, 2)))
                m = sum0[l] + BLOCKS * g + j
                if not known_below(m, 2):
                    pool.wait_ge(s_sum, done(m - 2))
                for r in range(RING):
                    e = RING * j + r
                    pool.wait_ge(s_scan, done(step(l, g, e)))
                    nc.gpsimd.tensor_tensor(hC[RING * odd + r][:, :], h[r][:, :], Ct[half][:, :], ALU.mult).then_inc(s_hC, 1)

            def between(l, p, buf, n):
                k = prep0[l] + p
                if n == 3:
                    pool.wait_ge(s_s, k + 1)
                    nc.gpsimd.tensor_tensor(delta[:, :], t_sum[:, :], t_relu[:, :], ALU.add).then_inc(s_delta, 1)
                    pool.wait_ge(s_x, 16 * (k + 1))
                    pool.wait_ge(s_delta, k + 1)
                    nc.gpsimd.tensor_tensor(dx[:, :], delta[:, :], xT[buf][:, :], ALU.mult).then_inc(s_dx, 1)

            def prologue(l):
                for n in range(SINGLE - 2):
                    between(l, 0, 0, n)
                step_block(l, 0, 0, 0, 0, 0)

            def half_body(l, g, half):
                half_steps(pool, l, g, half, step_block, between)
                if pair_mean[l]:
                    m = group0[l] + g
                    pool.wait_ge(s_store, 16 * m + 1)
                    pool.wait_ge(s_post, m + 2)
                    v = y_full[:, :].rearrange("p (t two) -> p t two", two=2)
                    nc.gpsimd.tensor_tensor(y_out[:, 0:W // 2], v[:, :, 0], v[:, :, 1], ALU.add).then_inc(s_yout, 1)

            for l in range(LAYERS):
                layer_loop(pool, l, prologue, half_body)


T3 = LENGTHS[2]
SEQS = W // T3
TOK = 124
NTOK = W // TOK
E_FFN, H_FFN = 32, 16
EXP_PER_TILE = P // (2 * H_FFN)
TILES = E_FFN // EXP_PER_TILE
TWO_PI = 6.283185307179586
C1 = 6.28125
C2 = 0.0019350051879882812
C3 = TWO_PI - C1 - C2
ROUND = 12582912.0
PI_LO = 3.1415925


def mixer_stage(nc, io, h3, out_dram, n_batch):
    chunks = n_batch // 2 // SEQS
    ctx = ExitStack()
    with ctx:
        def sb(name, shape, dt=FP32):
            return ctx.enter_context(nc.sbuf_tensor(name, shape, dt))

        def ps(name):
            return ctx.enter_context(nc.psum_tensor(name, [P, 2 * BANK], FP32))

        def sem(name):
            return ctx.enter_context(nc.semaphore(name))

        def wide(name, dt=FP32):
            return sb(name, [P, W], dt)

        loads = []

        def const(name, shape):
            t = sb("c_" + name, shape)
            loads.append((t, io[name]))
            return t

        mean_w = const("mean_w", [P, P])
        ident = const("ident", [P, P])
        b_re, b_im = const("b_re", [P, P]), const("b_im", [P, P])
        c_re, c_im = const("c_re", [P, P]), const("c_im", [P, P])
        s5c = const("s5c", [P, 4])
        times = const("times", [P, T3])
        rw, rb = const("rw", [P, 2 * E_FFN]), const("rb", [1, 2 * E_FFN])
        w1, b1 = const("w1", [P, TILES * P]), const("b1", [P, TILES])
        w2, b2 = const("w2", [P, TILES * P]), const("b2", [2 * E_FFN, P])
        expand_f = const("expand", [2 * E_FFN, TILES * P])
        rev = const("rev", [P, NTOK * 2 * E_FFN])
        expand = sb("expand_bf", [2 * E_FFN, TILES * P], BF16)
        ones = sb("ones_row", [1, P])
        eps = sb("eps", [P, 1])
        c_re2, c_re2n, c_im2n = sb("c_re2", [P, P]), sb("c_re2n", [P, P]), sb("c_im2n", [P, P])
        col = sb("s5_cols", [P, 24])
        ang, red, kk, cs, sn, half = [sb(f"s5_{n}", [P, T3]) for n in ("ang", "red", "k", "cos", "sin", "half")]
        t1r, t1i = sb("t1r", [P, T3]), sb("t1i", [P, T3])
        tt0, tt1 = sb("tt0", [P, T3]), sb("tt1", [P, T3])
        T1R, T1I, COS, SIN, DEC = [wide(n) for n in ("T1R", "T1I", "COS", "SIN", "DEC")]
        xcA, sqA, stA, rsA, uA = [wide(n) for n in ("xcA", "sqA", "stA", "rsA", "uA")]
        xcB, sqB, stB, rsB, uB = [wide(n) for n in ("xcB", "sqB", "stB", "rsB", "uB")]
        pr = [wide(f"pr{i}") for i in range(4)]
        wr, wi, zr, zi = [wide(n) for n in ("wr", "wi", "zr", "zi")]
        qq = [wide(f"qq{i}") for i in range(4)]
        res = wide("res")
        top, top2 = sb("top", [P, 2 * NTOK]), sb("top2", [P, 2 * NTOK])
        (eq, score), hot = [sb(n, [P, NTOK * 2 * E_FFN]) for n in ("eq", "score")], sb("hot", [P, (NTOK + 1) * 2 * E_FFN])
        hotT = sb("hotT", [2 * E_FFN, W])
        hotTb = sb("hotTb", [2 * E_FFN, W], BF16)
        relu = [wide(f"relu{i}") for i in range(2)]
        hid = [wide(f"hid{i}") for i in range(2)]
        fin = wide("fin")
        PA0, PA1, PB0, PB1 = ps("PA0"), ps("PA1"), ps("PB0"), ps("PB1")

        def banks(t, rows=P):
            return t[0:rows, :].rearrange("p (u c) -> p u c", u=2)[:, :, 0:UNIT]

        def flat(t):
            return t[:, :].rearrange("p (u c) -> p u c", u=2)

        def chunk(c):
            return h3[:, bass.ds(c * W, W)].rearrange("p (u c) -> p u c", u=2)

        s_load, s_set, s_tab, s_acol, s_abig = sem("c_loaded"), sem("consts_set"), sem("tables_step"), sem("cols_exp"), sem("sins")
        sA = {n: sem("A_" + n) for n in ("mean", "xc", "sq", "var", "std", "rstd", "u", "bu", "prod", "w", "z", "qpool", "qdve", "y", "t", "h")}
        sB = {n: sem("B_" + n) for n in ("mean", "xc", "sq", "var", "std", "rstd", "u", "logits", "pick", "hotT", "hotTcopy",
                                         "hid", "mask", "relu", "masked", "down", "fin", "out")}
        s_cn, s_chain, s_tables = sem("c_scaled"), sem("dve_chain"), sem("tables_done")
        s_bf = sem("expand_cast")
        block = ctx.enter_context(nc.Block())

        @block.sync
        def _(sp):
            for t, src in loads:
                sp.dma_start(t[:, :], src).then_inc(s_load, 16)
            with sp.Fori(0, chunks) as c:
                sp.wait_ge(sB["fin"], c + 2)
                sp.dma_start(out_dram[:, bass.ds(c * W, W)], fin[:, :]).then_inc(sB["out"], 16)
            sp.wait_ge(sB["out"], 16 * chunks + 1)

        @block.tensor
        def _(pe):
            pe.wait_ge(s_load, 16 * len(loads))
            pe.wait_ge(s_set, 2)
            pe.wait_ge(s_cn, 3)
            pe.wait_ge(s_bf, 1)

            def project(dst, wt, src, rows=P, start=True, stop=True):
                for n in range(2):
                    last = nc.tensor.matmul(banks(dst, rows)[:, n, :], wt, src[:, n, :], start=start, stop=stop)
                return last

            def mean(s, c, dst):
                if s is sB:
                    pe.wait_ge(sA["h"], c + 1)
                project(dst, mean_w[:, :], chunk(c)).then_inc(s["mean"], 1)

            def var(s, c, dst, sq):
                pe.wait_ge(s["sq"], c + 1)
                project(dst, mean_w[:, :], flat(sq)).then_inc(s["var"], 1)

            def a1(c):
                if not known_below(c, 1):
                    pe.wait_ge(sA["t"], c)
                mean(sA, c, PA0)

            def a2(c):
                var(sA, c, PA0, sqA)

            def a3(c):
                pe.wait_ge(sA["u"], c + 1)
                if not known_below(c, 1):
                    pe.wait_ge(sB["fin"], c)
                project(PA0, b_re[:, :], flat(uA))
                project(PA1, b_im[:, :], flat(uA)).then_inc(sA["bu"], 1)

            def a4(c):
                pe.wait_ge(sA["qpool"], 2 * c + 2)
                pe.wait_ge(sA["qdve"], 2 * c + 2)
                for n in range(2):
                    for i, wt in enumerate((c_re2, c_im2n, c_re2n, c_im2n)):
                        last = nc.tensor.matmul(banks(PA0)[:, n, :], wt[:, :], flat(qq[(0, 1, 3, 2)[i]])[:, n, :],
                                                start=(i == 0), stop=(i == 3))
                last.then_inc(sA["y"], 1)

            def b3(c):
                pe.wait_ge(sB["u"], c + 1)
                for j in range(NTOK):
                    dst = PB0[0:TOK, 2 * E_FFN * j:2 * E_FFN * (j + 1)]
                    nc.tensor.matmul(dst, ones[0:1, 0:TOK], rb[0:1, :], start=True, stop=False)
                    last = nc.tensor.matmul(dst, uB[:, TOK * j:TOK * (j + 1)], rw[:, :], start=False, stop=True)
                last.then_inc(sB["logits"], 1)

            def b4(c):
                pe.wait_ge(sB["pick"], 5 * c + 5)
                for j in range(NTOK):
                    n, m = divmod(j, NTOK // 2)
                    last = nc.tensor.transpose(PB1[:, BANK * n + TOK * m:BANK * n + TOK * (m + 1)],
                                               hot[0:TOK, 2 * E_FFN * j:2 * E_FFN * j + P], ident[0:TOK, 0:TOK])
                last.then_inc(sB["hotT"], 1)

            def b5(c, beside):
                pe.wait_ge(sB["hotTcopy"], 2 * c + 2)
                pe.wait_ge(sA["prod"], 4 * (c + 1) + (4 if beside else 0))
                project(PA1, b2[:, :], flat(hotT), stop=False)
                for k in range(TILES + 1):
                    if k < TILES:
                        if k:
                            pe.wait_ge(sB["relu"], TILES * c + k)
                        project(PB0, w1[:, P * k:P * (k + 1)], flat(uB)).then_inc(sB["hid"], 1)
                        if k:
                            pe.wait_ge(sB["masked"], TILES * c + k)
                        project(PB1, expand[:, P * k:P * (k + 1)], flat(hotTb)).then_inc(sB["mask"], 1)
                    if k:
                        pe.wait_ge(sB["masked"], TILES * c + k)
                        project(PA1, w2[:, P * (k - 1):P * k], flat(hid[(k - 1) % 2]), start=False,
                                stop=(k == TILES)).then_inc(sB["down"], 1)

            a1(0), a2(0), a3(0), a4(0)
            with pe.Fori(1, chunks) as i:
                a1(i)
                mean(sB, i - 1, PB0)
                a2(i)
                var(sB, i - 1, PB0, sqB)
                a3(i)
                b3(i - 1)
                b4(i - 1)
                a4(i)
                b5(i - 1, True)
            mean(sB, chunks - 1, PB0)
            var(sB, chunks - 1, PB0, sqB)
            b3(chunks - 1)
            b4(chunks - 1)
            b5(chunks - 1, False)

        @block.scalar
        def _(act):
            act.wait_ge(s_load, 16 * len(loads))
            nc.scalar.activation(col[:, 0:1], s5c[:, 2:3], ACT.Exp).then_inc(s_acol, 1)
            act.wait_ge(s_tab, 1)
            nc.scalar.activation(col[:, 3:4], col[:, 1:2], ACT.Exp).then_inc(s_acol, 1)
            nc.scalar.mul(c_re2[:, :], c_re[:, :], 2.0).then_inc(s_cn, 1)
            nc.scalar.mul(c_re2n[:, :], c_re[:, :], -2.0).then_inc(s_cn, 1)
            nc.scalar.mul(c_im2n[:, :], c_im[:, :], -2.0).then_inc(s_cn, 1)
            nc.scalar.copy(expand[:, :], expand_f[:, :]).then_inc(s_bf, 1)
            act.wait_ge(s_tab, 2)
            nc.scalar.activation(sn[:, :], red[:, :], ACT.Sin).then_inc(s_abig, 1)
            nc.scalar.activation(half[:, :], red[:, :], ACT.Sin, scale=0.5).then_inc(s_abig, 1)
            act.wait_ge(s_set, 2)

            def square(s, c, xc, sq):
                act.wait_ge(s["xc"], c + 1)
                nc.scalar.activation(sq[:, :], xc[:, :], ACT.Square).then_inc(s["sq"], 1)

            def std(s, c, src, dst):
                act.wait_ge(s["var"], c + 1)
                nc.scalar.activation(flat(dst), banks(src), ACT.Sqrt, bias=eps[:, 0:1]).then_inc(s["std"], 1)

            def b4(c):
                act.wait_ge(sB["hotT"], c + 1)
                src = banks(PB1, 2 * E_FFN)
                nc.scalar.copy(flat(hotT), src).then_inc(sB["hotTcopy"], 1)
                nc.scalar.copy(flat(hotTb), src).then_inc(sB["hotTcopy"], 1)

            def b5(c):
                for k in range(TILES):
                    act.wait_ge(sB["hid"], TILES * c + k + 1)
                    if k >= 2:
                        act.wait_ge(sB["masked"], TILES * c + k - 1)
                    nc.scalar.activation(flat(relu[k % 2]), banks(PB0), ACT.Relu, bias=b1[:, k:k + 1]).then_inc(sB["relu"], 1)

            square(sA, 0, xcA, sqA)
            std(sA, 0, PA0, stA)
            with act.Fori(1, chunks) as i:
                square(sA, i, xcA, sqA)
                square(sB, i - 1, xcB, sqB)
                std(sA, i, PA0, stA)
                std(sB, i - 1, PB0, stB)
                b4(i - 1)
                b5(i - 1)
            square(sB, chunks - 1, xcB, sqB)
            std(sB, chunks - 1, PB0, stB)
            b4(chunks - 1)
            b5(chunks - 1)

        @block.vector
        def _(dve):
            dve.sem_inc(sB["fin"], 1)
            nc.vector.memset(ones[:, :], 1.0).then_inc(s_set, 1)
            nc.vector.memset(hot[:, NTOK * 2 * E_FFN:], 0.0)
            nc.vector.memset(eps[:, :], 1e-5).then_inc(s_set, 1)
            dve.wait_ge(s_load, 16 * len(loads))
            seen = [0]

            def then(ins):
                seen[0] += 1
                ins.then_inc(s_chain, 1)
                dve.wait_ge(s_chain, seen[0])

            tt, ts, stt = nc.vector.tensor_tensor, nc.vector.tensor_scalar, nc.vector.scalar_tensor_tensor

            def cc(i):
                return col[:, i:i + 1]

            lre, lim = s5c[:, 0:1], s5c[:, 1:2]
            dve.wait_ge(s_acol, 1)
            tt(cc(1), lre, cc(0), ALU.mult).then_inc(s_tab, 1)
            then(tt(cc(2), lim, cc(0), ALU.mult))

            def reduce_angle(a, k, out):
                then(ts(k, a, 1.0 / TWO_PI, ROUND, ALU.mult, ALU.add))
                then(ts(k, k, ROUND, None, ALU.subtract))
                then(stt(out, k, -C1, a, ALU.mult, ALU.add))
                then(stt(out, k, -C2, out, ALU.mult, ALU.add))
                then(stt(out, k, -C3, out, ALU.mult, ALU.add))

            reduce_angle(cc(2), cc(4), cc(5))
            then(ts(cc(6), cc(5), ROUND / 4096.0, ROUND / 4096.0, ALU.add, ALU.subtract))
            then(tt(cc(7), cc(5), cc(6), ALU.subtract))
            then(ts(ang[:, :], times[:, :], cc(6), None, ALU.mult))
            reduce_angle(ang[:, :], kk[:, :], red[:, :])
            then(stt(red[:, :], times[:, :], cc(7), red[:, :], ALU.mult, ALU.add))
            ts(red[:, :], red[:, :], PI_LO, -PI_LO, ALU.min, ALU.max).then_inc(s_tab, 1)
            dve.wait_ge(s_abig, 2)
            then(tt(cs[:, :], half[:, :], half[:, :], ALU.mult))
            then(ts(cs[:, :], cs[:, :], -2.0, 1.0, ALU.mult, ALU.add))
            dve.wait_ge(s_acol, 2)
            then(tt(cc(8), cc(3), cs[:, 1:2], ALU.mult))
            then(ts(cc(8), cc(8), -1.0, None, ALU.add))
            then(tt(cc(9), cc(3), sn[:, 1:2], ALU.mult))
            then(tt(cc(10), lre, lre, ALU.mult))
            then(stt(cc(10), lim, lim, cc(10), ALU.mult, ALU.add))
            then(nc.vector.reciprocal(cc(11), cc(10)))
            then(tt(cc(12), cc(9), lim, ALU.mult))
            then(stt(cc(12), cc(8), lre, cc(12), ALU.mult, ALU.add))
            then(tt(cc(13), cc(8), lim, ALU.mult))
            then(stt(cc(13), cc(9), lre, cc(13), ALU.mult, ALU.subtract))
            then(tt(cc(14), cc(12), cc(11), ALU.mult))
            then(tt(cc(15), cc(13), cc(11), ALU.mult))
            then(ts(tt0[:, :], sn[:, :], cc(15), None, ALU.mult))
            then(stt(t1r[:, :], cs[:, :], cc(14), tt0[:, :], ALU.mult, ALU.add))
            then(ts(tt1[:, :], sn[:, :], cc(14), None, ALU.mult))
            then(stt(t1i[:, :], cs[:, :], cc(15), tt1[:, :], ALU.mult, ALU.subtract))

            def seqs(t):
                return t[:, :].rearrange("p (s t) -> p s t", s=SEQS)

            for dst, src in ((T1R, t1r), (T1I, t1i), (COS, cs), (SIN, sn)):
                nc.vector.tensor_copy(seqs(dst), src[:, :].unsqueeze(1).broadcast_to([P, SEQS, T3]))
            then(nc.vector.memset(DEC[:, :], 0.0))
            then(ts(seqs(DEC)[:, :, 1:], seqs(COS)[:, :, 1:], 0.0, cc(3), ALU.mult, ALU.add))
            nc.vector.memset(top[:, 0:1], 0.0).then_inc(s_tables, 1)

            def center(s, c, src, xc):
                dve.wait_ge(s["mean"], c + 1)
                tt(flat(xc), chunk(c), banks(src), ALU.subtract).then_inc(s["xc"], 1)

            def scale(s, c, st, rs, xc, out):
                dve.wait_ge(s["std"], c + 1)
                nc.vector.reciprocal(rs[:, :], st[:, :]).then_inc(s["rstd"], 1)
                dve.wait_ge(s["rstd"], c + 1)
                tt(out[:, :], xc[:, :], rs[:, :], ALU.mult).then_inc(s["u"], 1)

            def a3(c):
                dve.wait_ge(sA["bu"], c + 1)
                for i, (bank, table) in enumerate(((PA0, T1R), (PA1, T1I), (PA0, T1I), (PA1, T1R))):
                    tt(flat(pr[i]), banks(bank), flat(table), ALU.mult).then_inc(sA["prod"], 1)

            def a3b(c):
                dve.wait_ge(sA["w"], 2 * c + 1)
                nc.vector.tensor_tensor_scan(zr[:, :], DEC[:, :], wr[:, :], 0.0, ALU.mult, ALU.add).then_inc(sA["z"], 1)
                dve.wait_ge(sA["w"], 2 * c + 2)
                nc.vector.tensor_tensor_scan(zi[:, :], DEC[:, :], wi[:, :], 0.0, ALU.mult, ALU.add).then_inc(sA["z"], 1)
                dve.wait_ge(sA["z"], 2 * c + 2)
                tt(qq[2][:, :], zi[:, :], COS[:, :], ALU.mult).then_inc(sA["qdve"], 1)
                tt(qq[3][:, :], zi[:, :], SIN[:, :], ALU.mult).then_inc(sA["qdve"], 1)

            def a4(c):
                dve.wait_ge(sA["y"], c + 1)
                stt(flat(res), flat(uA), s5c[:, 3:4], banks(PA0), ALU.mult, ALU.add).then_inc(sA["t"], 1)
                dve.wait_ge(sA["t"], c + 1)
                tt(chunk(c), chunk(c), flat(res), ALU.add).then_inc(sA["h"], 1)

            def b3(c):
                dve.wait_ge(sB["logits"], c + 1)
                shape = [TOK, 2 * NTOK, E_FFN]
                lg = PB0[0:TOK, 0:2 * E_FFN * NTOK].rearrange("p (j e) -> p j e", e=E_FFN)

                def e3(t):
                    return t[0:TOK, :].rearrange("p (j e) -> p j e", e=E_FFN)

                def over(t):
                    return t[0:TOK, :].unsqueeze(2).broadcast_to(shape)

                n = 5 * c
                nc.vector.reduce_max(top[0:TOK, :], lg, mybir.AxisListType.X).then_inc(sB["pick"], 1)
                dve.wait_ge(sB["pick"], n + 1)
                tt(e3(eq), lg, over(top), ALU.is_equal).then_inc(sB["pick"], 1)
                dve.wait_ge(sB["pick"], n + 2)
                tt(score[0:TOK, :], eq[0:TOK, :], rev[0:TOK, :], ALU.mult).then_inc(sB["pick"], 1)
                dve.wait_ge(sB["pick"], n + 3)
                nc.vector.reduce_max(top2[0:TOK, :], e3(score), mybir.AxisListType.X).then_inc(sB["pick"], 1)
                dve.wait_ge(sB["pick"], n + 4)
                tt(e3(hot[:, 0:NTOK * 2 * E_FFN]), e3(score), over(top2), ALU.is_equal).then_inc(sB["pick"], 1)

            def b5(c):
                for k in range(TILES):
                    dve.wait_ge(sB["relu"], TILES * c + k + 1)
                    dve.wait_ge(sB["mask"], TILES * c + k + 1)
                    if k >= 2:
                        dve.wait_ge(sB["down"], TILES * c + k - 1)
                    tt(flat(hid[k % 2]), banks(PB1), flat(relu[k % 2]), ALU.mult).then_inc(sB["masked"], 1)
                dve.wait_ge(sB["down"], TILES * c + TILES)
                dve.wait_ge(sB["out"], 16 * c + 1)
                stt(flat(fin), banks(PA1), 0.0, chunk(c), ALU.max, ALU.add).then_inc(sB["fin"], 1)

            center(sA, 0, PA0, xcA)
            scale(sA, 0, stA, rsA, xcA, uA)
            a3(0), a3b(0), a4(0)
            with dve.Fori(1, chunks) as i:
                center(sA, i, PA0, xcA)
                center(sB, i - 1, PB0, xcB)
                scale(sA, i, stA, rsA, xcA, uA)
                scale(sB, i - 1, stB, rsB, xcB, uB)
                a3(i)
                b3(i - 1)
                a3b(i)
                a4(i)
                b5(i - 1)
            center(sB, chunks - 1, PB0, xcB)
            scale(sB, chunks - 1, stB, rsB, xcB, uB)
            b3(chunks - 1)
            b5(chunks - 1)

        @block.gpsimd
        def _(pool):
            pool.sem_inc(sB["out"], 1)
            pool.wait_ge(s_tables, 1)

            def a3(c):
                tt = nc.gpsimd.tensor_tensor
                pool.wait_ge(sA["prod"], 4 * c + 2)
                tt(wr[:, :], pr[0][:, :], pr[1][:, :], ALU.subtract).then_inc(sA["w"], 1)
                pool.wait_ge(sA["prod"], 4 * c + 4)
                tt(wi[:, :], pr[2][:, :], pr[3][:, :], ALU.add).then_inc(sA["w"], 1)
                pool.wait_ge(sA["z"], 2 * c + 1)
                tt(qq[0][:, :], zr[:, :], COS[:, :], ALU.mult).then_inc(sA["qpool"], 1)
                tt(qq[1][:, :], zr[:, :], SIN[:, :], ALU.mult).then_inc(sA["qpool"], 1)

            with pool.Fori(0, chunks) as c:
                a3(c)


def _lay_out(x):
    import numpy as np

    f = np.float32
    n = x["x"].shape[0]
    xt = x["x"][:, :UNIT].reshape(n // 4, 2, 2, UNIT, D).transpose(0, 4, 2, 1, 3).reshape(n // 4, P, W)
    out = {"x": np.concatenate([xt, np.zeros((1, P, W), f)]).transpose(1, 0, 2).reshape(P, -1)}

    def per_batch(w, by_b_in=False, by_b_out=False):
        z = np.zeros(w.shape[:-2] + ((2, w.shape[-2]) if by_b_in else (w.shape[-2], 2))
                     + ((2, w.shape[-1]) if by_b_out else (w.shape[-1], 2)), f)
        for b in range(2):
            at = (Ellipsis,) + ((b, slice(None)) if by_b_in else (slice(None), b)) + ((b, slice(None)) if by_b_out else (slice(None), b))
            z[at] = w
        return z.reshape(w.shape[:-2] + (2 * w.shape[-2], 2 * w.shape[-1]))

    wd = x["L0_tok_W_dbc"]
    out["wdt"] = per_batch(np.repeat(wd[:, 0, :, None], D, 2))
    out["wB"] = per_batch(wd[:, 1:1 + NS].transpose(0, 2, 1), by_b_out=True)
    out["wC"] = per_batch(wd[:, 1 + NS:].transpose(0, 2, 1), by_b_out=True)
    a_log = x["L0_tok_A_log"].reshape(LAYERS, NQ, EPQ, NS).transpose(0, 3, 2, 1).reshape(LAYERS, NS, D)
    out["a_log"] = np.tile(a_log, (1, 2, 1))
    cols = np.stack([x["L0_tok_W_dt"][:, :, 0], x["L0_tok_b_dt"], x["L0_tok_D"]], 1)
    out["cols"] = np.repeat(cols.reshape(3 * LAYERS, D).T, 2, 0)
    spread = np.zeros((PARTS + 1, EPQ, 2, EPQ, 2, NS), f)
    gather = np.zeros((2, P, 2 * QR - 2), f)
    for b in range(2):
        for r in range(EPQ):
            spread[:PARTS, r, b, r, b, :] = 1.0
        gather[0, NS * b:NS * (b + 1), QR - 2 + b] = 0.5
        gather[1, NS * b:NS * (b + 1), QR - 2 + b] = 1.0
    out["spread"] = spread.reshape(P, EPQ * P)
    out["gather"] = gather

    out["mean_w"] = per_batch(np.full((D, D), 1.0 / D, f))
    out["ident"] = np.eye(P, dtype=f)
    bb, cc = x["L0_attn_B"], x["L0_attn_C"]
    out["b_re"], out["b_im"] = per_batch(bb[:, :, 0].T), per_batch(bb[:, :, 1].T)
    out["c_re"], out["c_im"] = per_batch(cc[:, :, 0].T), per_batch(cc[:, :, 1].T)
    s5 = np.stack([x["L0_attn_Lambda_re"], x["L0_attn_Lambda_im"], x["L0_attn_log_step"][:, 0], x["L0_attn_D"]], 1)
    out["s5c"] = np.repeat(s5, 2, 0)
    out["times"] = np.tile(np.arange(T3, dtype=f), (P, 1))
    out["rw"] = per_batch(x["L0_ffn_router_w"].T, by_b_out=True)
    out["rb"] = np.tile(x["L0_ffn_router_b"], 2).reshape(1, -1)
    w1 = x["L0_ffn_W1"].transpose(1, 0, 2).reshape(D, TILES, EXP_PER_TILE * H_FFN).transpose(1, 0, 2)
    out["w1"] = per_batch(w1).transpose(1, 0, 2).reshape(P, TILES * P)
    out["b1"] = np.repeat(x["L0_ffn_b1"].reshape(TILES, EXP_PER_TILE * H_FFN).T, 2, 0)
    w2 = x["L0_ffn_W2"].reshape(TILES, EXP_PER_TILE * H_FFN, D)
    out["w2"] = per_batch(w2).transpose(1, 0, 2).reshape(P, TILES * P)
    out["b2"] = per_batch(x["L0_ffn_b2"], by_b_in=True)
    expand = np.zeros((E_FFN, TILES, EXP_PER_TILE, H_FFN), f)
    for e in range(E_FFN):
        expand[e, e // EXP_PER_TILE, e % EXP_PER_TILE] = 1.0
    out["expand"] = per_batch(expand.reshape(E_FFN, E_FFN * H_FFN), by_b_in=True)
    out["rev"] = np.tile(np.arange(E_FFN, 0, -1).astype(f), (P, 2 * NTOK))
    return {k: np.ascontiguousarray(v) for k, v in out.items()}


def build(nc, io, out_dram, n_batch):
    layer1_groups = n_batch * LENGTHS[1] // (2 * W)
    with nc.sbuf_tensor("h_store", [P, (layer1_groups + 1) * W], FP32) as h3:
        ssm_stage(nc, io, h3, n_batch)
        mixer_stage(nc, io, h3, out_dram, n_batch)


def kernel(**inputs):
    import numpy as np
    import concourse.bacc as bacc
    from concourse.bass_utils import run_bass_kernel_spmd

    n_batch = inputs["x"].shape[0]
    arrays = {f"in_{k}": v for k, v in _lay_out({k: np.asarray(v) for k, v in inputs.items()}).items()}
    nc = bacc.Bacc("TRN2", target_bir_lowering=False, num_devices=1)
    io = {k[3:]: nc.dram_tensor(k, v.shape, FP32, kind="ExternalInput").ap() for k, v in arrays.items()}
    out = nc.dram_tensor("out_h", (P, n_batch // 2 * T3), FP32, kind="ExternalOutput").ap()
    build(nc, io, out, n_batch)
    got = run_bass_kernel_spmd(nc, [arrays], core_ids=[0]).results[0]["out_h"]
    return got.reshape(D, 2, n_batch // 2, T3).transpose(2, 1, 3, 0).reshape(n_batch, T3, D)
```
